# Optimizing a Trainium2 kernel written in Bass

```python
import numpy as np
import jax
import jax.numpy as jnp

def _softmax(x, axis=-1):
    return jax.nn.softmax(x, axis=axis)

def _gelu(x):
    return jax.nn.gelu(x, approximate=True)

def _silu(x):
    return jax.nn.silu(x)

def _sigmoid(x):
    return jax.nn.sigmoid(x)

def _layernorm(x, axis=-1, eps=1e-05):
    m = jnp.mean(x, axis=axis, keepdims=True)
    v = jnp.var(x, axis=axis, keepdims=True)
    return (x - m) / jnp.sqrt(v + eps)

def _scatter_add(tgt, idx, src, axis=0):
    return tgt.at[idx].add(src)

def _segment_sum(src, seg, n):
    return jax.ops.segment_sum(src, seg, n)
kernel_name = 'mk_gnn_resnorm_d2_gnn_r8_7038e7'

def setup_inputs(seed: int=0):
    np.random.seed(seed)
    _w = jnp.asarray

    def _rec_inputs():
        import jax
        import jax.numpy as jnp
        _gk = jax.random.key(seed)
        x = -0.000202 + 1 * jax.random.normal(jax.random.fold_in(_gk, 1), (12500, 64), jnp.float32)
        src = jax.random.randint(jax.random.fold_in(_gk, 2), (200000,), 0, 12500, jnp.int32)
        dst = jnp.minimum((12500 * jax.random.uniform(jax.random.fold_in(_gk, 3), (200000,)) ** 2.0).astype(jnp.int32), 99999)
        _o = jnp.argsort(dst, stable=True)
        src = src[_o]
        dst = dst[_o]
        edge_type_16 = jax.random.randint(jax.random.fold_in(_gk, 13), (200000,), 0, 16, jnp.int32)
        return (x, src, dst, edge_type_16)
    x, src, dst, edge_type_16 = _rec_inputs()

    def _L0_gnn_setup():
        import jax, jax.numpy as jnp
        import numpy as np
        N = 12500
        E = 100000
        D = 64
        H = 2
        F = 64
        L = 3
        SLOPE = 0.2

        def _gat_layer(x, src, dst, W, b, a, Wr):
            xl = (x @ W + b).reshape(-1, H, F)
            s = jax.nn.leaky_relu(xl[dst] + xl[src], SLOPE)
            logits = jnp.einsum('ehf,hf->eh', s, a)
            m = jax.ops.segment_max(logits, dst, num_segments=N)
            ex = jnp.exp(logits - m[dst])
            denom = jax.ops.segment_sum(ex, dst, num_segments=N)
            alpha = ex / denom[dst]
            out = jax.ops.segment_sum(xl[src] * alpha[:, :, None], dst, num_segments=N)
            out = out + (x @ Wr)[:, None, :]
            out = jax.nn.elu(out)
            return out.mean(axis=1)
        key = jax.random.key(seed)
        ks = jax.random.split(key, 6)
        x = jax.random.normal(ks[0], (N, D), dtype=jnp.float32)
        edge_index = jax.random.randint(ks[1], (2, E), 0, N, dtype=jnp.int64)
        W = jax.random.normal(ks[2], (L, D, H * F), dtype=jnp.float32) / np.sqrt(D)
        b = jnp.zeros((L, H * F), dtype=jnp.float32)
        attn = jax.random.normal(ks[3], (L, H, F), dtype=jnp.float32) / np.sqrt(F)
        Wr = jax.random.normal(ks[4], (L, D, F), dtype=jnp.float32) / np.sqrt(D)
        return {'x': x, 'edge_index': edge_index, 'W': W, 'b': b, 'attn': attn, 'Wr': Wr}
    _L0_gnn_all = _L0_gnn_setup()
    _L0_gnn_in = {k: v for k, v in _L0_gnn_all.items() if k in ('W', 'b', 'attn', 'Wr')}
    del _L0_gnn_all

    def _L1_gnn_setup():
        import jax, jax.numpy as jnp
        import numpy as np
        N_NODES = 12500
        N_EDGES = 125000
        D_IN = 64
        D_OUT = 64
        N_RELS = 16
        key = jax.random.key(seed)
        k1, k2, k3, k4, k5 = jax.random.split(key, 5)
        feat = jax.random.normal(k1, (N_NODES, D_IN), dtype=jnp.float32)
        weight = jax.random.normal(k2, (N_RELS, D_IN, D_OUT), dtype=jnp.float32) * 0.05
        src = jax.random.randint(k3, (N_EDGES,), 0, N_NODES)
        dst = jax.random.randint(k4, (N_EDGES,), 0, N_NODES)
        etypes = jax.random.randint(k5, (N_EDGES,), 0, N_RELS)
        return {'feat': feat, 'weight': weight, 'src': src, 'dst': dst, 'etypes': etypes}
    _L1_gnn_all = _L1_gnn_setup()
    _L1_gnn_in = {k: v for k, v in _L1_gnn_all.items() if k in ('weight',)}
    del _L1_gnn_all
    return {'x': x, 'src': src, 'dst': dst, 'edge_type_16': edge_type_16, 'L0_gnn_W': _L0_gnn_in['W'], 'L0_gnn_b': _L0_gnn_in['b'], 'L0_gnn_attn': _L0_gnn_in['attn'], 'L0_gnn_Wr': _L0_gnn_in['Wr'], 'L1_gnn_weight': _L1_gnn_in['weight']}

def reference(x, src, dst, edge_type_16, L0_gnn_W, L0_gnn_b, L0_gnn_attn, L0_gnn_Wr, L1_gnn_weight):
    import jax
    import jax.numpy as jnp

    def _L0_gnn_ref(x, edge_index, W, b, attn, Wr):
        import jax, jax.numpy as jnp
        import numpy as np
        N = 12500
        E = 100000
        D = 64
        H = 2
        F = 64
        L = 3
        SLOPE = 0.2

        def _gat_layer(x, src, dst, W, b, a, Wr):
            xl = (x @ W + b).reshape(-1, H, F)
            s = jax.nn.leaky_relu(xl[dst] + xl[src], SLOPE)
            logits = jnp.einsum('ehf,hf->eh', s, a)
            m = jax.ops.segment_max(logits, dst, num_segments=N)
            ex = jnp.exp(logits - m[dst])
            denom = jax.ops.segment_sum(ex, dst, num_segments=N)
            alpha = ex / denom[dst]
            out = jax.ops.segment_sum(xl[src] * alpha[:, :, None], dst, num_segments=N)
            out = out + (x @ Wr)[:, None, :]
            out = jax.nn.elu(out)
            return out.mean(axis=1)
        src, dst = (edge_index[0], edge_index[1])
        h = x
        for l in range(L):
            h = _gat_layer(h, src, dst, W[l], b[l], attn[l], Wr[l])
        return h

    def _L1_gnn_ref(feat, weight, src, dst, etypes):
        import jax, jax.numpy as jnp
        import numpy as np
        N_NODES = 12500
        N_EDGES = 125000
        D_IN = 64
        D_OUT = 64
        N_RELS = 16
        h = feat[src]
        n_rels = weight.shape[0]
        e, d_out = (h.shape[0], weight.shape[2])

        def step(m, rw):
            r, w_r = rw
            mask = jnp.where(etypes == r, 1.0, 0.0).astype(h.dtype)
            m = m + mask[:, None] * (h @ w_r)
            return (m, None)
        m0 = jnp.zeros((e, d_out), dtype=h.dtype)
        m, _ = jax.lax.scan(step, m0, (jnp.arange(n_rels), weight))
        out = jax.ops.segment_sum(m, dst, num_segments=feat.shape[0])
        return out
    edge_index = jnp.stack([src, dst])
    x = _layernorm(x + _L0_gnn_ref(x, edge_index, L0_gnn_W, L0_gnn_b, L0_gnn_attn, L0_gnn_Wr), axis=-1)
    x = _layernorm(x + _L1_gnn_ref(x, L1_gnn_weight, src, dst, edge_type_16), axis=-1)
    return x

_drawn_inputs = setup_inputs


def setup_inputs(seed=0):
    import zlib

    import numpy as np

    out = dict(_drawn_inputs(seed))
    spreads = {'L0_gnn_b': (0.0, 0.1)}
    factors = {}
    for name, (base, spread) in spreads.items():
        noise = np.random.default_rng([zlib.crc32(name.encode()), seed]).standard_normal(out[name].shape)
        drawn = base * np.exp(spread * noise) if base else spread * noise
        out[name] = jnp.asarray(drawn.astype(out[name].dtype))
    for name, factor in factors.items():
        out[name] = (out[name] * factor).astype(out[name].dtype)
    return out
```

```python
from contextlib import ExitStack

import concourse.bass as bass
from concourse import mybir

ALU = mybir.AluOpType
ACT = mybir.ActivationFunctionType
F32 = mybir.dt.float32
BF16 = mybir.dt.bfloat16
I32 = mybir.dt.int32
AX_X = mybir.AxisListType.X

P = 128
NODES, EDGES, D = 12500, 200000, 64
HEADS, LAYERS, RELS = 2, 3, 16
HF = HEADS * D
WINDOWS = -(-NODES // P)
LAST = NODES - (WINDOWS - 1) * P
BINS = WINDOWS + 1
PAD_NODE = WINDOWS * P
COLS = 1565
TILES = 5
RANK_GROUPS = COLS // TILES
GROUP = 8
SLOTS = 1664
GROUPS = SLOTS // GROUP
REC = 4
BIG = float(2.0 ** 100)
assert (EDGES - WINDOWS) // P + WINDOWS + -(-(P * COLS - EDGES) // P) <= SLOTS
assert COLS % TILES == 0 and RANK_GROUPS % 2 == 1 and TILES * BINS <= 512


def constants(nc, k):
    with nc.semaphore("iota_done") as iota_done, nc.semaphore("made") as made, nc.Block() as block:
        @block.gpsimd
        def _(pool):
            nc.gpsimd.iota(k["col"][:, :], [[1, P]], base=0, channel_multiplier=0,
                           allow_small_or_imprecise_dtypes=True).then_inc(iota_done, 1)
            nc.gpsimd.iota(k["lane"][:, :], [[0, 1]], base=0, channel_multiplier=1,
                           allow_small_or_imprecise_dtypes=True).then_inc(iota_done, 1)
            nc.gpsimd.iota(k["slot_id"][:, :], [[1, SLOTS // P]], base=0, channel_multiplier=SLOTS // P,
                           allow_small_or_imprecise_dtypes=True).then_inc(iota_done, 1)

        @block.vector
        def _(dve):
            nc.vector.memset(k["ones"][:, :], 1.0).then_inc(made, 1)
            nc.vector.memset(k["ones_bf"][:, :], 1.0).then_inc(made, 1)
            dve.wait_ge(iota_done, 3)
            nc.vector.tensor_scalar(k["ident"][:, :], k["col"][:, :], k["lane"][:, 0:1], None, ALU.is_equal).then_inc(made, 1)
            nc.vector.tensor_scalar(k["ident_bf"][:, :], k["col"][:, :], k["lane"][:, 0:1], None, ALU.is_equal).then_inc(made, 1)
            nc.vector.tensor_scalar(k["before"][:, :], k["col"][:, :], k["lane"][:, 0:1], None, ALU.is_gt).then_inc(made, 1)
            nc.vector.tensor_copy(k["col_bf"][:, :], k["col"][:, :]).then_inc(made, 1)
            dve.wait_ge(made, 6)


def order_edges(nc, k, src, dst, rel, recs, wtab_dram, wtab):
    with ExitStack() as ctx:
        def sb(name, shape, dt):
            return ctx.enter_context(nc.sbuf_tensor(name, shape, dt))

        def ps(name, shape, dt=F32):
            return ctx.enter_context(nc.psum_tensor(name, shape, dt))

        def sem(name):
            return ctx.enter_context(nc.semaphore(name))

        ids = sb("ids", [P, 3, COLS], I32)
        rec = sb("rec", [P, COLS, REC], I32)
        tmp = sb("tmp", [P, COLS], I32)
        win = sb("win", [P, COLS], BF16)
        junk = sb("junk", [P, COLS], BF16)
        blank = sb("blank", [P, SLOTS, REC], I32)
        below = sb("below", [P, BINS + 1], F32)
        total = sb("total", [P, BINS + 1], F32)
        count = sb("count", [P, BINS], I32)
        whole = sb("whole", [P, BINS], I32)
        wholef = sb("wholef", [P, BINS], F32)
        upto = sb("upto", [P, BINS], F32)
        base = sb("base", [P, 2, BINS], F32)
        wcol = sb("wcol", [P, SLOTS // P], F32)
        wcoli = sb("wcoli", [P, SLOTS // P], I32)
        wjunk = sb("wjunk", [P, BINS], F32)
        hot = sb("hot", [P, 2, TILES, BINS], BF16)
        rank = sb("rank", [P, 2, TILES, BINS], F32)
        pos = sb("pos", [P, 2, TILES], F32)
        posi = sb("posi", [P, 2, TILES], I32)
        lane8 = sb("lane8", [P, 2, TILES], I32)
        slot8 = sb("slot8", [P, 2, TILES], I32)
        grp = sb("grp", [P, 2, TILES], I32)
        addr = sb("addr", [P, 2, TILES], I32)
        recst = sb("recst", [P, 2, TILES * REC], I32)
        ps_rank = [ps(f"ps_rank{i}", [P, TILES, BINS]) for i in range(2)]
        ps_sum = [ps(f"ps_sum{i}", [P, BINS]) for i in range(2)]
        ps_total = ps("ps_total", [P, BINS + 1])

        pads_set, loaded, blank_set, blanks_stored = sem("pads_set"), sem("loaded"), sem("blank_set"), sem("blanks_stored")
        counted, totals_ready = sem("counted"), sem("totals_ready")
        chain = sem("chain")
        wtab_ready, wtab_stored, wtab_loaded = sem("wtab_ready"), sem("wtab_stored"), sem("wtab_loaded")
        hot_ready, ranked, rank_read = sem("hot_ready"), sem("ranked"), sem("rank_read")
        step = sem("step")
        addr_ready = sem("addr_ready")
        rec_ready = sem("rec_ready")
        scatter_begun = sem("scatter_begun")
        scattered = [sem(f"scattered{b}") for b in range(2)]
        block = ctx.enter_context(nc.Block())
        full = P - 1

        @block.sync
        def _(sp):
            sp.wait_ge(pads_set, 3)
            for n, a in enumerate((src, dst, rel)):
                sp.dma_start(ids[0:full, n, :], a[0:full * COLS].rearrange("(p c) -> p c", c=COLS)).then_inc(loaded, 16)
                sp.dma_start(ids[full:P, n, 0:EDGES - full * COLS],
                             a[full * COLS:EDGES].rearrange("(p c) -> p c", p=1)).then_inc(loaded, 16)
            sp.wait_ge(blank_set, 4)
            sp.dma_start(recs.rearrange("(p s) r -> p (s r)", p=P), blank[:, :, :].rearrange("p s r -> p (s r)")).then_inc(blanks_stored, 16)
            sp.wait_ge(wtab_ready, 1)
            sp.dma_start(wtab_dram.rearrange("(p s) -> p s", p=P), wcoli[:, :]).then_inc(wtab_stored, 16)
            sp.wait_ge(wtab_stored, 16)
            sp.dma_start(wtab[0:1, :], wtab_dram.rearrange("(p s) -> p s", p=1)).then_inc(wtab_loaded, 16)
            sp.wait_ge(wtab_loaded, 16)

        @block.tensor
        def _(pe):
            pe.wait_ge(counted, BINS + 1)
            nc.tensor.matmul(ps_total[:, :], k["ones"][:, :], below[:, :], start=True, stop=True).then_inc(totals_ready, 1)

            def ranks(g, b, first):
                pe.wait_ge(hot_ready, g + 1)
                if not first:
                    pe.wait_ge(rank_read, g - 1)
                nc.tensor.matmul(ps_rank[b][:, :, :], k["before"][:, :], hot[:, b, :, :], start=True, stop=False, skip_group_check=True)
                for i in range(TILES - 1):
                    nc.tensor.matmul(ps_rank[b][:, i + 1:TILES, :], k["ones_bf"][:, :],
                                     hot[:, b, i:i + 1, :].to_broadcast([P, TILES - 1 - i, BINS]),
                                     start=False, stop=(i == TILES - 2), skip_group_check=True)
                for i in range(TILES):
                    last = nc.tensor.matmul(ps_sum[b][:, :], k["ones_bf"][:, :], hot[:, b, i, :], start=(i == 0), stop=(i == TILES - 1))
                last.then_inc(ranked, 1)

            ranks(0, 0, True)
            ranks(1, 1, True)
            with pe.Fori(1, RANK_GROUPS // 2) as n:
                for b in range(2):
                    ranks(n * 2 + b, b, False)
            ranks(RANK_GROUPS - 1, 0, False)

        @block.vector
        def _(dve):
            nc.vector.memset(ids[:, 0, :], PAD_NODE).then_inc(pads_set, 1)
            nc.vector.memset(ids[:, 1, :], PAD_NODE).then_inc(pads_set, 1)
            nc.vector.memset(ids[:, 2, :], 0).then_inc(pads_set, 1)
            nc.vector.memset(blank[:, :, 0], PAD_NODE).then_inc(blank_set, 1)
            nc.vector.memset(blank[:, :, 1].bitcast(F32), -1.0).then_inc(blank_set, 1)
            nc.vector.memset(blank[:, :, 2], PAD_NODE * RELS).then_inc(blank_set, 1)
            nc.vector.memset(blank[:, :, 3], 0).then_inc(blank_set, 1)
            nc.vector.memset(rec[:, :, 3], 0).then_inc(chain, 1)
            dve.wait_ge(loaded, 96)
            nc.vector.tensor_scalar(tmp[:, :], ids[:, 1, :], 7, None, ALU.logical_shift_right).then_inc(chain, 1)
            dve.wait_ge(chain, 2)
            nc.vector.tensor_copy(win[:, :], tmp[:, :]).then_inc(chain, 1)
            dve.wait_ge(chain, 3)
            with dve.Fori(0, BINS + 1) as w:
                nc.vector.tensor_scalar(junk[:, :], win[:, :], k["col"][:, bass.ds(w, 1)], None, ALU.is_lt, ALU.add,
                                        accum_out=below[:, bass.ds(w, 1)]).then_inc(counted, 1)
                dve.wait_ge(counted, w + 1)
            nc.vector.tensor_scalar(tmp[:, :], ids[:, 1, :], P - 1, None, ALU.bitwise_and).then_inc(chain, 1)
            dve.wait_ge(chain, 4)
            nc.vector.tensor_copy(rec[:, :, 1].bitcast(F32), tmp[:, :]).then_inc(chain, 1)
            dve.wait_ge(chain, 5)
            nc.vector.tensor_copy(rec[:, :, 0], ids[:, 0, :]).then_inc(chain, 1)
            nc.vector.tensor_scalar(tmp[:, :], ids[:, 0, :], 4, None, ALU.logical_shift_left).then_inc(chain, 1)
            dve.wait_ge(chain, 7)
            nc.vector.tensor_tensor(rec[:, :, 2], tmp[:, :], ids[:, 2, :], ALU.add).then_inc(rec_ready, 1)
            dve.wait_ge(totals_ready, 1)
            nc.vector.tensor_copy(total[:, :], ps_total[:, :]).then_inc(chain, 1)
            dve.wait_ge(chain, 8)
            nc.vector.scalar_tensor_tensor(out=count[:, :], in0=total[:, 1:BINS + 1], scalar=float(P - 1), in1=total[:, 0:BINS],
                                           op0=ALU.add, op1=ALU.subtract).then_inc(chain, 1)
            dve.wait_ge(chain, 9)
            nc.vector.tensor_scalar(whole[:, :], count[:, :], 7, None, ALU.logical_shift_right).then_inc(chain, 1)
            dve.wait_ge(chain, 10)
            nc.vector.tensor_copy(wholef[:, :], whole[:, :]).then_inc(chain, 1)
            dve.wait_ge(chain, 11)
            nc.vector.tensor_tensor_scan(upto[:, :], k["ones"][:, 0:BINS], wholef[:, :], 0.0, ALU.mult, ALU.add).then_inc(chain, 1)
            dve.wait_ge(chain, 12)
            nc.vector.tensor_tensor(wjunk[:, :], upto[:, :], wholef[:, :], ALU.subtract).then_inc(chain, 1)
            dve.wait_ge(chain, 13)
            nc.vector.tensor_scalar(base[:, 0, :], wjunk[:, :], float(P), None, ALU.mult).then_inc(chain, 1)
            dve.wait_ge(chain, 14)
            for j in range(SLOTS // P):
                nc.vector.tensor_scalar(wjunk[:, :], upto[:, :], k["slot_id"][:, j:j + 1], None, ALU.is_le, ALU.add,
                                        accum_out=wcol[:, j:j + 1]).then_inc(chain, 1)
                dve.wait_ge(chain, 15 + j)
            nc.vector.tensor_scalar(wcoli[:, :], wcol[:, :], float(BINS - 1), None, ALU.min).then_inc(wtab_ready, 1)

            def one_hot(g, b, first):
                if not first:
                    dve.wait_ge(ranked, g - 1)
                    dve.wait_ge(step, (g - 1) * 9)
                off = g * TILES
                w = win[:, bass.ds(off, TILES)].unsqueeze(2).to_broadcast([P, TILES, BINS])
                c = k["col_bf"][:, 0:BINS].unsqueeze(1).to_broadcast([P, TILES, BINS])
                nc.vector.tensor_tensor(hot[:, b, :, :], c, w, ALU.is_equal).then_inc(hot_ready, 1)

            def place(g, b, first):
                s = g * 9
                dve.wait_ge(ranked, g + 1)
                if not first:
                    dve.wait_ge(step, s)
                nc.vector.tensor_tensor(rank[:, b, :, :], ps_rank[b][:, :, :],
                                        base[:, b, :].unsqueeze(1).to_broadcast([P, TILES, BINS]), ALU.add).then_inc(step, 1)
                nc.vector.tensor_tensor(base[:, 1 - b, :], ps_sum[b][:, :], base[:, b, :], ALU.add).then_inc(step, 1)
                dve.wait_ge(step, s + 2)
                nc.vector.tensor_tensor(rank[:, b, :, :], rank[:, b, :, :], hot[:, b, :, :], ALU.mult).then_inc(rank_read, 1)
                dve.wait_ge(rank_read, g + 1)
                nc.vector.tensor_reduce(pos[:, b, :], rank[:, b, :, :], AX_X, ALU.add).then_inc(step, 1)
                dve.wait_ge(step, s + 3)
                nc.vector.tensor_copy(posi[:, b, :], pos[:, b, :]).then_inc(step, 1)
                dve.wait_ge(step, s + 4)
                nc.vector.tensor_scalar(lane8[:, b, :], posi[:, b, :], P - 1, 3, ALU.bitwise_and, ALU.logical_shift_left).then_inc(step, 1)
                nc.vector.tensor_scalar(slot8[:, b, :], posi[:, b, :], 7, GROUP - 1, ALU.logical_shift_right, ALU.bitwise_and).then_inc(step, 1)
                nc.vector.tensor_scalar(grp[:, b, :], posi[:, b, :], 10, 10, ALU.logical_shift_right, ALU.logical_shift_left).then_inc(step, 1)
                dve.wait_ge(step, s + 7)
                nc.vector.tensor_tensor(slot8[:, b, :], slot8[:, b, :], lane8[:, b, :], ALU.bitwise_or).then_inc(step, 1)
                dve.wait_ge(step, s + 8)
                if not first:
                    dve.wait_ge(scattered[b], uses(g))
                nc.vector.tensor_tensor(addr[:, b, :], slot8[:, b, :], grp[:, b, :], ALU.bitwise_or).then_inc(step, 1)
                nc.vector.tensor_copy(recst[:, b, :], rec[:, bass.ds(g * TILES, TILES), :].rearrange("p t r -> p (t r)")).then_inc(addr_ready, 1)

            def uses(g):
                return (g // 2) * (16 * TILES)

            dve.wait_ge(rec_ready, 1)
            one_hot(0, 0, True)
            one_hot(1, 1, True)
            place(0, 0, True)
            place(1, 1, True)
            with dve.Fori(1, RANK_GROUPS // 2) as n:
                for b in range(2):
                    one_hot(n * 2 + b, b, False)
                for b in range(2):
                    place(n * 2 + b, b, False)
            one_hot(RANK_GROUPS - 1, 0, False)
            place(RANK_GROUPS - 1, 0, False)

        @block.gpsimd
        def _(pool):
            pool.wait_ge(blanks_stored, 16)

            def scatter(g, b):
                pool.wait_ge(addr_ready, g + 1)
                pool.wait_ge(step, (g + 1) * 9)
                pool.sem_inc(scatter_begun, 1)
                for t in range(TILES):
                    nc.gpsimd.indirect_dma_start(
                        recs, bass.IndirectOffsetOnAxis(ap=addr[:, b, t:t + 1], axis=0),
                        recst[:, b, t * REC:(t + 1) * REC], None).then_inc(scattered[b], 16)

            scatter(0, 0)
            scatter(1, 1)
            with pool.Fori(1, RANK_GROUPS // 2) as n:
                for b in range(2):
                    scatter(n * 2 + b, b)
            scatter(RANK_GROUPS - 1, 0)
            pool.wait_ge(scattered[0], 16 * TILES * (RANK_GROUPS // 2 + 1))
            pool.wait_ge(scattered[1], 16 * TILES * (RANK_GROUPS // 2))


def attention_layers(nc, k, t, x, W, bias, attn, Wr, recs, table, wtab):
    with ExitStack() as ctx:
        def sb(name, shape, dt=F32):
            return ctx.enter_context(nc.sbuf_tensor(name, shape, dt))

        def sem(name):
            return ctx.enter_context(nc.semaphore(name))

        h, acc, xls, banks = t["h"], t["acc"], t["xls"], t["banks"]
        negmax = sb("negmax", [P, BINS * HEADS])
        wcat = sb("wcat", [P, 2, HF + D])
        brow = sb("brow", [1, HF])
        acol = sb("acol", [P, 1])
        a2 = sb("a2", [P, HEADS])
        arep = sb("arep", [P, HEADS, P])
        hs = sb("hs", [P, 2, 2 * D])
        hT = sb("hT", [P, 2, P])
        xl32 = sb("xl32", [P, 2, 2, HF])
        rest = sb("rest", [P, 2, 2, HF])
        rec = sb("rec_in", [P, 2, GROUP, REC], I32)
        xs = sb("xs", [P, 8, HF])
        hot = sb("hot_e", [P, 4, 4, P])
        hotT = sb("hotT", [P, 2, 4 * P])
        maskT = sb("maskT", [P, 2, 4, P], BF16)
        z02 = sb("z02", [P, 2, P])
        zl = sb("zl", [P, 4, P])
        tmax = sb("tmax", [P, 2, HEADS])
        nmb = sb("nmb", [P, 4, HEADS])
        dif = sb("dif", [P, 2, HEADS])
        corr = sb("corr", [P, 4, HEADS])
        msg = sb("msg", [P, 2, HEADS, D + 1])
        rden = sb("rden", [P, WINDOWS, HEADS])

        ps_z = [banks[i][:, 0:P] for i in range(2)]
        ps_l = [banks[2 + i][:, 0:HEADS * P].rearrange("p (h e) -> p h e", h=HEADS) for i in range(2)]
        ps_s = [banks[4 + i][:, 0:HEADS * (D + 1)].rearrange("p (h f) -> p h f", h=HEADS) for i in range(2)]
        ps_d = banks[6][:, 0:HEADS]
        ps_hot = banks[7][:, :].bitcast(BF16)[:, 0:4 * P]
        ps_hT = [banks[i][:, 0:P] for i in range(2)]
        ps_y = [banks[2 + i][:, 0:2 * (HF + D)].rearrange("p (a f) -> p a f", a=2) for i in range(2)]

        weights_loaded, a_ready, zeroed, cleared = sem("weights_loaded"), sem("a_ready"), sem("zeroed"), sem("cleared")
        hs_ready, hT_ps, hT_ready, y_ready = sem("hs_ready"), sem("hT_ps"), sem("hT_ready"), sem("y_ready")
        y_kept, y_split = sem("y_kept"), sem("y_split")
        xl_ready, stored, split = sem("xl_ready"), [sem("stored0"), sem("stored1")], sem("split")
        zero_row, wcat_zero = sem("zero_row"), sem("wcat_zero")
        rec_loaded = [sem("rec_loaded0"), sem("rec_loaded1")]
        gathered = [sem(f"gathered{i}") for i in range(8)]
        gather_begun = sem("gather_begun")
        hot_ready, hotT_ps, hotT_ready = sem("hot_ready_e"), sem("hotT_ps"), sem("hotT_ready")
        z_ready, z02_ready, zl_ready, logits_ready = sem("z_ready"), sem("z02_ready"), sem("zl_ready"), sem("logits_ready")
        tile_max, nm_ready, dif_ready, max_saved = sem("tile_max"), sem("nm_ready"), sem("dif_ready"), sem("max_saved")
        d_ready, p_ready, c_ready, msg_ready = sem("d_ready"), sem("p_ready"), sem("c_ready"), sem("msg_ready")
        s_ready, acc_done = sem("s_ready"), sem("acc_done")
        fin, elu_in, elu_exp, node_done = sem("fin"), sem("elu_in"), sem("elu_exp"), sem("node_done")
        block = ctx.enter_context(nc.Block())

        PAIRS = WINDOWS // 2
        QUADS = SLOTS // 4
        STEPS = SLOTS + 3
        BODY = 16
        ONE = {"skip_group_check": True}

        def windows(engine, first, count):
            _, values = nc.values_load_multi_w_load_instructions(
                wtab[0:1, bass.ds(first, count)], engines=[engine], min_val=0, max_val=BINS - 1,
                skip_runtime_bounds_check_because="the window of a slot is counted over BINS windows and capped there")
            return values

        def steps(eng, l, step):
            for i in range(BODY):
                step(0, i, l)
            with eng.Fori(1, SLOTS // BODY - 1) as n:
                for i in range(BODY):
                    step(n * BODY, i, l)
            for i in range(BODY):
                step(SLOTS - BODY, i, l)
            for i in range(STEPS - SLOTS):
                step(SLOTS, i, l)

        @block.sync
        def _(sp):
            sp.wait_ge(wcat_zero, 1)
            with sp.Fori(0, LAYERS) as l:
                sp.wait_ge(node_done, l)
                for a in range(2):
                    half = slice(a * D, a * D + D)
                    sp.dma_start(wcat[half, a, 0:HF], W[bass.ds(l, 1)].rearrange("l d f -> (l d) f")).then_inc(weights_loaded, 16)
                    sp.dma_start(wcat[half, a, HF:HF + D], Wr[bass.ds(l, 1)].rearrange("l d f -> (l d) f")).then_inc(weights_loaded, 16)
                sp.dma_start(brow[0:1, :], bias[bass.ds(l, 1), :]).then_inc(weights_loaded, 16)
                with nc.allow_non_contiguous_dma(reason="128 numbers, one for each lane"):
                    sp.dma_start(acol[:, 0:1], attn[bass.ds(l, 1)].rearrange("l h f -> (h f) l")).then_inc(weights_loaded, 16)

                def store(j, b):
                    sp.wait_ge(xl_ready, l * PAIRS + j + 1)
                    sp.dma_start(table[bass.ds(j * 2 * P, 2 * P), :].rearrange("(a p) f -> p a f", a=2),
                                 xl32[:, b, :, :]).then_inc(stored[b], 16)

                store(0, 0)
                with sp.Fori(0, PAIRS // 2) as n:
                    store(n * 2 + 1, 1)
                    store(n * 2 + 2, 0)

                def load(g, b, first):
                    if not first:
                        sp.wait_ge(msg_ready, l * SLOTS + (g - 1) * GROUP)
                    sp.dma_start(rec[:, b, :, :].rearrange("p s r -> p (s r)"),
                                 recs[bass.ds(g * GROUP * P, GROUP * P), :].rearrange("(p s) r -> p (s r)", s=GROUP)).then_inc(rec_loaded[b], 16)

                load(0, 0, True)
                load(1, 1, True)
                with sp.Fori(1, GROUPS // 2) as n:
                    for b in range(2):
                        load(n * 2 + b, b, False)

        @block.gpsimd
        def _(pool):
            nc.gpsimd.memset(t["zeros"][0:1, :], 0.0).then_inc(zeroed, 1)
            pool.wait_ge(zeroed, 1)
            pool.dma_start(table[PAD_NODE:PAD_NODE + 1, :], t["zeros"][0:1, 0:HF]).then_inc(zero_row, 16)
            pool.wait_ge(zero_row, 16)
            with pool.Fori(0, LAYERS) as l:
                pool.wait_ge(stored[0], (l + 1) * (16 * (PAIRS // 2 + 1)))
                pool.wait_ge(stored[1], (l + 1) * (16 * (PAIRS // 2)))

                def gather(q, i, first):
                    if not first:
                        pool.wait_ge(msg_ready, l * SLOTS + (q - 1) * 4)
                    if i % 2 == 0:
                        pool.wait_ge(rec_loaded[i // 2 % 2], l * (16 * GROUPS // 2) + (q // 4 * 16 + 16))
                    pool.sem_inc(gather_begun, 1)
                    for s in range(4):
                        slot = i % 2 * 4 + s
                        nc.gpsimd.indirect_dma_start(
                            xs[:, slot, :], None, table,
                            bass.IndirectOffsetOnAxis(ap=rec[:, i // 2 % 2, slot, 0:1], axis=0)).then_inc(gathered[slot], 16)

                for i in range(4):
                    gather(i, i, i < 2)
                with pool.Fori(1, QUADS // 4) as n:
                    for i in range(4):
                        gather(n * 4 + i, i, False)

        @block.tensor
        def _(pe):
            with pe.Fori(0, LAYERS) as l:
                def turn(j, b):
                    pe.wait_ge(hs_ready, l * PAIRS + j + 1)
                    nc.tensor.transpose(ps_hT[b], hs[:, b, :], k["ident"][:, :]).then_inc(hT_ps, 1)

                def project(j, b, first):
                    pe.wait_ge(hT_ready, l * PAIRS + j + 1)
                    if not first:
                        pe.wait_ge(y_kept, l * PAIRS + j - 1)
                    nc.tensor.matmul(ps_y[b][:, :, 0:HF], k["ones"][0:1, :],
                                     brow[0:1, :].unsqueeze(1).to_broadcast([1, 2, HF]), start=True, stop=False, **ONE)
                    nc.tensor.matmul(ps_y[b][:, :, :], hT[:, b, :], wcat[:, :, :], start=False, stop=True, **ONE).then_inc(y_ready, 1)

                pe.wait_ge(weights_loaded, l * 96 + 96)
                turn(0, 0)
                turn(1, 1)
                project(0, 0, True)
                turn(2, 0)
                project(1, 1, True)
                with pe.Fori(1, PAIRS // 2) as n:
                    turn(n * 2 + 1, 1)
                    project(n * 2, 0, False)
                    turn(n * 2 + 2, 0)
                    project(n * 2 + 1, 1, False)
                project(PAIRS - 1, 0, False)

                pe.wait_ge(a_ready, l * 4 + 4)
                values = {}

                def turn_hot(first, q, l):
                    pe.wait_ge(hot_ready, l * QUADS + first // 4 + q + 1)
                    pe.wait_ge(hotT_ready, (l * QUADS + first // 4 + q) * 2)
                    for s in range(4):
                        last = nc.tensor.transpose(ps_hot[:, s * P:s * P + P],
                                                   hot[:, q % 4, s, :].bitcast(BF16)[:, 1:2 * P:2], k["ident_bf"][:, :])
                    last.then_inc(hotT_ps, 1)

                def step(first, i, l):
                    g = l * SLOTS + first + i
                    static = isinstance(first, int)
                    at = first + i if static else 99
                    if at < SLOTS:
                        if i % 4 == 0:
                            values["w"] = windows(mybir.EngineType.PE, first + i, 4)
                            pe.wait_ge(hotT_ready, (l * QUADS + (first + i) // 4 + 1) * 2 if static else (l * QUADS + first // 4 + (i // 4 + 1)) * 2)
                        w = values["w"][i % 4]
                        if at >= 2:
                            pe.wait_ge(zl_ready, g - 1)
                        pe.wait_ge(gathered[i % 8], l * (16 * SLOTS // 8) + (first * 2 + (i // 8 + 1) * 16))
                        nc.tensor.matmul(ps_z[i % 2], xs[:, i % 8, :], k["ident"][:, :], start=True, stop=False)
                        pair = hotT[:, i // 4 % 2, i % 4 * P:i % 4 * P + P].bitcast(BF16)[:, 1:2 * P:2]
                        for part in range(3):
                            last = nc.tensor.matmul(ps_z[i % 2], xls[:, bass.ds(w * (3 * HF) + part * HF, HF)], pair,
                                                    start=False, stop=(part == 2))
                        last.then_inc(z_ready, 1)
                        if i % 4 == 1 and (not static or at + 3 < SLOTS):
                            turn_hot(first, i // 4 + 1, l)
                    if 1 <= at and (not static or 0 <= first + i - 1 < SLOTS):
                        j = (i - 1) % BODY
                        pe.wait_ge(zl_ready, g)
                        if at >= 3:
                            pe.wait_ge(tile_max, g - 2)
                        nc.tensor.matmul(ps_l[j % 2], k["ident_bf"][:, :],
                                         maskT[:, j // 4 % 2, j % 4:j % 4 + 1, :].to_broadcast([P, HEADS, P]), start=True, stop=False, **ONE)
                        for hd in range(HEADS):
                            last = nc.tensor.matmul(ps_l[j % 2][:, hd, :], arep[:, hd, :], zl[:, j % 4, :], start=False, stop=(hd == 1), **ONE)
                        last.then_inc(logits_ready, 1)
                    if 2 <= at and (not static or 0 <= first + i - 2 < SLOTS):
                        j = (i - 2) % BODY
                        pe.wait_ge(nm_ready, g - 1)
                        if at >= 3:
                            pe.wait_ge(p_ready, g - 2)
                        nc.tensor.matmul(ps_d, zl[:, j % 4, :], a2[:, :], start=True, stop=False)
                        nc.tensor.matmul(ps_d, hotT[:, j // 4 % 2, j % 4 * P:j % 4 * P + P], nmb[:, j % 4, :],
                                         start=False, stop=True).then_inc(d_ready, 1)
                    if 3 <= at and (not static or 0 <= first + i - 3 < SLOTS):
                        j = (i - 3) % BODY
                        pe.wait_ge(msg_ready, g - 2)
                        if at >= 5:
                            pe.wait_ge(acc_done, (g - 4) * 2)
                        nc.tensor.matmul(ps_s[j % 2], hot[:, j // 4, j % 4, :], msg[:, j % 2, :, :], start=True, stop=True).then_inc(s_ready, 1)

                turn_hot(0, 0, l)
                steps(pe, l, step)

        @block.scalar
        def _(act):
            with act.Fori(0, LAYERS) as l:
                def rows(j, b, first):
                    if not first:
                        act.wait_ge(hT_ps, l * PAIRS + j - 1)
                    nc.scalar.activation(hs[:, b, :], h[:, bass.ds(j * (2 * D), 2 * D)], ACT.Copy).then_inc(hs_ready, 1)

                def turned(j, b, first):
                    act.wait_ge(hT_ps, l * PAIRS + j + 1)
                    if not first:
                        act.wait_ge(y_ready, l * PAIRS + j - 1)
                    nc.scalar.activation(hT[:, b, :], ps_hT[b], ACT.Copy).then_inc(hT_ready, 1)

                def keep(j, b, first):
                    act.wait_ge(y_ready, l * PAIRS + j + 1)
                    if not first:
                        n = PAIRS // 2 + 1 if b == 0 else PAIRS // 2
                        act.wait_ge(stored[b], l * (16 * n) + (j // 2) * 16)
                        act.wait_ge(split, l * (3 * PAIRS + 1) + (j * 3 - 2))
                    nc.scalar.activation(xl32[:, b, :, :], ps_y[b][:, :, 0:HF], ACT.Copy).then_inc(xl_ready, 1)
                    nc.scalar.activation(h[:, bass.ds(j * (2 * D), 2 * D)].rearrange("p (a f) -> p a f", a=2),
                                         ps_y[b][:, :, HF:HF + D], ACT.Copy).then_inc(y_kept, 1)

                act.wait_ge(node_done, l)
                rows(0, 0, True)
                turned(0, 0, True)
                rows(1, 1, True)
                turned(1, 1, True)
                keep(0, 0, True)
                rows(2, 0, False)
                turned(2, 0, False)
                keep(1, 1, True)
                with act.Fori(1, PAIRS // 2) as n:
                    for o, b in ((1, 1), (2, 0)):
                        rows(n * 2 + o, b, False)
                        turned(n * 2 + o, b, False)
                        keep(n * 2 + (o - 1), 1 - b, False)
                keep(PAIRS - 1, 0, False)

                def masks(first, q, l):
                    act.wait_ge(hotT_ps, l * QUADS + first // 4 + q + 1)
                    if not (isinstance(first, int) and first // 4 + q < 2):
                        act.wait_ge(d_ready, l * SLOTS + first + (q - 1) * 4)
                    nc.scalar.activation(hotT[:, q % 2, :], ps_hot, ACT.Copy).then_inc(hotT_ready, 1)
                    nc.scalar.activation(maskT[:, q % 2, :, :].rearrange("p s e -> p (s e)"), ps_hot, ACT.Copy,
                                         scale=BIG, bias=-BIG).then_inc(hotT_ready, 1)

                def step(first, i, l):
                    g = l * SLOTS + first + i
                    static = isinstance(first, int)
                    at = first + i if static else 99
                    if at < SLOTS:
                        act.wait_ge(z_ready, g + 1)
                        if at >= 2:
                            act.wait_ge(zl_ready, g - 1)
                        nc.scalar.activation(z02[:, i % 2, :], ps_z[i % 2], ACT.Copy, scale=0.2).then_inc(z02_ready, 1)
                        if i % 4 == 2 and (not static or at + 2 < SLOTS):
                            masks(first, i // 4 + 1, l)
                    if 2 <= at and (not static or 0 <= first + i - 2 < SLOTS):
                        j = (i - 2) % BODY
                        act.wait_ge(d_ready, g - 1)
                        if at >= 4:
                            act.wait_ge(s_ready, g - 3)
                        nc.scalar.activation(msg[:, j % 2, :, D], ps_d, ACT.Exp).then_inc(p_ready, 1)
                    if 1 <= at and (not static or 0 <= first + i - 1 < SLOTS):
                        j = (i - 1) % BODY
                        act.wait_ge(dif_ready, g)
                        if at >= 5:
                            act.wait_ge(acc_done, (g - 4) * 2)
                        nc.scalar.activation(corr[:, j % 4, :], dif[:, j % 2, :], ACT.Exp).then_inc(c_ready, 1)

                masks(0, 0, l)
                steps(act, l, step)
                act.wait_ge(elu_in, l + 1)
                low = xls[:, :].bitcast(F32)[:, 0:WINDOWS * HF]
                nc.scalar.activation(low, low, ACT.Exp).then_inc(elu_exp, 1)

        @block.vector
        def _(dve):
            nc.vector.memset(wcat[:, :, :], 0.0).then_inc(wcat_zero, 1)
            nc.vector.memset(a2[:, :], 0.0).then_inc(cleared, 1)
            nc.vector.memset(arep[:, :, :], 0.0).then_inc(cleared, 1)
            dve.wait_ge(cleared, 2)
            with dve.Fori(0, LAYERS) as l:
                nc.vector.memset(xls[:, WINDOWS * 3 * HF:BINS * 3 * HF], 0.0).then_inc(split, 1)
                dve.wait_ge(weights_loaded, l * 96 + 96)
                for hd in range(HEADS):
                    half = slice(hd * D, hd * D + D)
                    nc.vector.tensor_copy(a2[half, hd:hd + 1], acol[half, 0:1]).then_inc(a_ready, 1)
                    nc.vector.tensor_copy(arep[half, hd, :], acol[half, 0:1].to_broadcast([D, P])).then_inc(a_ready, 1)

                def parts(j, b):
                    hi, mid, lo = [xls[:, bass.ds(j * (6 * HF), 6 * HF)].rearrange("p (a s f) -> p a s f", a=2, s=3)[:, :, n, :] for n in range(3)]
                    dve.wait_ge(xl_ready, l * PAIRS + j + 1)
                    nc.vector.tensor_scalar(hi, xl32[:, b, :, :], 1.0, None, ALU.mult).then_inc(split, 1)
                    dve.wait_ge(split, (l * PAIRS + j) * 3 + (l + 2))
                    nc.vector.tensor_tensor(rest[:, b, :, :], xl32[:, b, :, :], hi, ALU.subtract).then_inc(y_split, 1)
                    dve.wait_ge(y_split, l * PAIRS + j + 1)
                    nc.vector.tensor_scalar(mid, rest[:, b, :, :], 1.0, None, ALU.mult).then_inc(split, 1)
                    dve.wait_ge(split, (l * PAIRS + j) * 3 + (l + 3))
                    nc.vector.tensor_tensor(lo, rest[:, b, :, :], mid, ALU.subtract).then_inc(split, 1)

                parts(0, 0)
                with dve.Fori(0, PAIRS // 2) as n:
                    parts(n * 2 + 1, 1)
                    parts(n * 2 + 2, 0)
                dve.wait_ge(split, (l + 1) * (3 * PAIRS + 1))
                nc.vector.memset(acc[:, :], 0.0).then_inc(cleared, 1)
                nc.vector.memset(negmax[:, :], BIG).then_inc(cleared, 1)
                dve.wait_ge(cleared, l * 2 + 4)
                values = {}

                def one_hots(first, q, l):
                    b = q // 2 % 2
                    dve.wait_ge(rec_loaded[b], l * (16 * GROUPS // 2) + (first + 16 * (q // 4 + 1)))
                    if not (isinstance(first, int) and first // 4 + q < 4):
                        dve.wait_ge(s_ready, l * SLOTS + first + (q - 3) * 4)
                    place = rec[:, b, q % 2 * 4:q % 2 * 4 + 4, 1:2].bitcast(F32).to_broadcast([P, 4, P])
                    nc.vector.tensor_tensor(hot[:, q % 4, :, :], k["col"][:, :].unsqueeze(1).to_broadcast([P, 4, P]), place,
                                            ALU.is_equal).then_inc(hot_ready, 1)

                def step(first, i, l):
                    g = l * SLOTS + first + i
                    static = isinstance(first, int)
                    at = first + i if static else 99

                    def has(back):
                        return not static or 0 <= first + i - back < SLOTS

                    if i % 4 == 0:
                        back = 0 if at == 0 else 3
                        count = 3 if at == 0 else 6
                        if static and at >= SLOTS:
                            count = 3
                        values[i // 4] = (-back, windows(mybir.EngineType.DVE, first + (i - back), count))
                    base, ws = values[i // 4]

                    def w(back):
                        return ws[i % 4 - back - base]

                    jr, jm, ja = (i - 1) % BODY, (i - 2) % BODY, (i - 3) % BODY
                    if has(1):
                        dve.wait_ge(logits_ready, g)
                        if at >= 3:
                            dve.wait_ge(nm_ready, g - 2)
                        nc.vector.tensor_reduce(tmax[:, jr % 2, :], ps_l[jr % 2], AX_X, ALU.max).then_inc(tile_max, 1)
                    if has(0):
                        dve.wait_ge(z02_ready, g + 1)
                        if at >= 4:
                            dve.wait_ge(d_ready, g - 3)
                        nc.vector.tensor_tensor(zl[:, i % 4, :], ps_z[i % 2], z02[:, i % 2, :], ALU.max).then_inc(zl_ready, 1)
                    if has(1):
                        nm = negmax[:, bass.ds(w(1) * HEADS, HEADS)]
                        dve.wait_ge(tile_max, g)
                        if at >= 2:
                            dve.wait_ge(max_saved, g - 1)
                        if at >= 5:
                            dve.wait_ge(d_ready, g - 4)
                        nc.vector.scalar_tensor_tensor(out=nmb[:, jr % 4, :], in0=tmax[:, jr % 2, :], scalar=-1.0, in1=nm,
                                                       op0=ALU.mult, op1=ALU.min).then_inc(nm_ready, 1)
                    if has(2):
                        dve.wait_ge(p_ready, g - 1)
                        nc.vector.tensor_tensor(msg[:, jm % 2, :, 0:D], xs[:, jm % 8, :].rearrange("p (h f) -> p h f", h=HEADS),
                                                msg[:, jm % 2, :, D:D + 1].to_broadcast([P, HEADS, D]), ALU.mult).then_inc(msg_ready, 1)
                    if has(1):
                        dve.wait_ge(nm_ready, g)
                        if at >= 3:
                            dve.wait_ge(c_ready, g - 2)
                        nc.vector.tensor_tensor(dif[:, jr % 2, :], nmb[:, jr % 4, :], nm, ALU.subtract).then_inc(dif_ready, 1)
                    if has(3):
                        dve.wait_ge(s_ready, g - 2)
                        dve.wait_ge(c_ready, g - 2)
                        if at >= 4:
                            dve.wait_ge(acc_done, (g - 3) * 2)
                        for hd in range(HEADS):
                            a = acc[:, bass.ds(w(3) * (HEADS * (D + 1)) + hd * (D + 1), D + 1)]
                            nc.vector.scalar_tensor_tensor(out=a, in0=a, scalar=corr[:, ja % 4, hd:hd + 1], in1=ps_s[ja % 2][:, hd, :],
                                                           op0=ALU.mult, op1=ALU.add).then_inc(acc_done, 1)
                    if has(1):
                        dve.wait_ge(dif_ready, g)
                        nc.vector.tensor_scalar(nm, nmb[:, jr % 4, :], 1.0, None, ALU.mult).then_inc(max_saved, 1)
                    if i % 4 == 0 and (not static or at + 4 < SLOTS):
                        one_hots(first, i // 4 + 1, l)

                one_hots(0, 0, l)
                steps(dve, l, step)

                av = acc[:, 0:WINDOWS * HEADS * (D + 1)].rearrange("p (w h f) -> p w h f", w=WINDOWS, h=HEADS)
                low = xls[:, :].bitcast(F32)[:, 0:WINDOWS * HF].rearrange("p (w h f) -> p w h f", w=WINDOWS, h=HEADS)
                hv = h[:, :].rearrange("p (w f) -> p w f", f=D)
                num = av[:, :, :, 0:D]
                dve.wait_ge(acc_done, (l + 1) * (2 * SLOTS))
                nc.vector.tensor_scalar(rden[:, :, :], av[:, :, :, D], 1e-30, None, ALU.max).then_inc(fin, 1)
                dve.wait_ge(fin, l * 6 + 1)
                nc.vector.reciprocal(rden[:, :, :], rden[:, :, :]).then_inc(fin, 1)
                dve.wait_ge(fin, l * 6 + 2)
                nc.vector.tensor_tensor(num, num, rden[:, :, :].unsqueeze(3).to_broadcast([P, WINDOWS, HEADS, D]), ALU.mult).then_inc(fin, 1)
                dve.wait_ge(fin, l * 6 + 3)
                nc.vector.tensor_tensor(num, num, hv.unsqueeze(2).to_broadcast([P, WINDOWS, HEADS, D]), ALU.add).then_inc(fin, 1)
                dve.wait_ge(fin, l * 6 + 4)
                nc.vector.tensor_scalar(low, num, 0.0, None, ALU.min).then_inc(elu_in, 1)
                dve.wait_ge(elu_exp, l + 1)
                nc.vector.scalar_tensor_tensor(out=low.rearrange("p w h f -> p (w h) f"), in0=num.rearrange("p w h f -> p (w h) f"), scalar=0.0,
                                               in1=low.rearrange("p w h f -> p (w h) f"), op0=ALU.max, op1=ALU.add).then_inc(fin, 1)
                dve.wait_ge(fin, l * 6 + 5)
                nc.vector.tensor_tensor(hv, low[:, :, 0, :], low[:, :, 1, :], ALU.add).then_inc(fin, 1)
                dve.wait_ge(fin, l * 6 + 6)
                nc.vector.tensor_scalar(hv, hv, 1.0 / HEADS, -1.0, ALU.mult, ALU.add).then_inc(node_done, 1)
            dve.wait_ge(node_done, LAYERS)


def load_nodes(nc, x, xt):
    with nc.semaphore("x_set") as x_set, nc.semaphore("x_loaded") as x_loaded, nc.Block() as block:
        @block.vector
        def _(dve):
            nc.vector.memset(xt[:, (WINDOWS - 1) * D:WINDOWS * D], 0.0).then_inc(x_set, 1)

        @block.sync
        def _(sp):
            sp.wait_ge(x_set, 1)
            rows = (WINDOWS - 1) * P
            for w in range(0, WINDOWS - 1, 25):
                n = min(25, WINDOWS - 1 - w)
                sp.dma_start(xt[:, w * D:(w + n) * D].rearrange("p (w f) -> p w f", f=D),
                             x[w * P:(w + n) * P, :].rearrange("(w p) f -> p w f", p=P)).then_inc(x_loaded, 16)
            sp.dma_start(xt[0:LAST, (WINDOWS - 1) * D:WINDOWS * D], x[rows:NODES, :]).then_inc(x_loaded, 16)
            sp.wait_ge(x_loaded, 16 * 5)


def normed(nc, dve, v, sq, stat, eps_var, std, done):
    wide = [P, WINDOWS, D]
    nc.vector.tensor_reduce(stat[:, 0, :], v, AX_X, ALU.add).then_inc(done, 1)
    dve.wait_ge(done, 2)
    nc.vector.tensor_scalar(stat[:, 0, :], stat[:, 0, :], 1.0 / D, None, ALU.mult).then_inc(done, 1)
    dve.wait_ge(done, 3)
    nc.vector.tensor_tensor(v, v, stat[:, 0, :].unsqueeze(2).to_broadcast(wide), ALU.subtract).then_inc(done, 1)
    dve.wait_ge(done, 4)
    nc.vector.tensor_tensor(sq, v, v, ALU.mult).then_inc(done, 1)
    dve.wait_ge(done, 5)
    nc.vector.tensor_reduce(stat[:, 1, :], sq, AX_X, ALU.add).then_inc(done, 1)
    dve.wait_ge(done, 6)
    nc.vector.tensor_scalar(stat[:, 1, :], stat[:, 1, :], 1.0 / D, 1e-5, ALU.mult, ALU.add).then_inc(eps_var, 1)
    dve.wait_ge(std, 1)
    nc.vector.reciprocal(stat[:, 1, :], stat[:, 1, :]).then_inc(done, 1)
    dve.wait_ge(done, 7)
    nc.vector.tensor_tensor(v, v, stat[:, 1, :].unsqueeze(2).to_broadcast(wide), ALU.mult).then_inc(done, 1)
    dve.wait_ge(done, 8)


def node_rows(dram, tile):
    parts = []
    for w in range(0, WINDOWS - 1, 25):
        n = min(25, WINDOWS - 1 - w)
        parts.append((dram[w * P:(w + n) * P, :].rearrange("(w p) f -> p w f", p=P), tile[:, w:w + n, :]))
    parts.append((dram[(WINDOWS - 1) * P:NODES, :], tile[0:LAST, WINDOWS - 1, :]))
    return parts


def residual_norm(nc, t, x):
    with (
        nc.sbuf_tensor("stat", [P, 2, WINDOWS], F32) as stat, nc.semaphore("x_set2") as x_set, nc.semaphore("x_again") as x_again,
        nc.semaphore("norm_done") as done, nc.semaphore("var_ready") as var_ready, nc.semaphore("std_ready") as std_ready,
        nc.Block() as block,
    ):
        xt = t["acc"][:, 0:WINDOWS * D].rearrange("p (w f) -> p w f", f=D)
        sq = t["xls"][:, :].bitcast(F32)[:, 0:WINDOWS * D].rearrange("p (w f) -> p w f", f=D)
        v = t["h"][:, :].rearrange("p (w f) -> p w f", f=D)
        parts = node_rows(x, xt)

        @block.sync
        def _(sp):
            sp.wait_ge(x_set, 1)
            for rows, tile in parts:
                sp.dma_start(tile, rows).then_inc(x_again, 16)

        @block.vector
        def _(dve):
            nc.vector.memset(xt[:, WINDOWS - 1, :], 0.0).then_inc(x_set, 1)
            dve.wait_ge(x_again, 16 * len(parts))
            nc.vector.tensor_tensor(v, v, xt, ALU.add).then_inc(done, 1)
            dve.wait_ge(done, 1)
            normed(nc, dve, v, sq, stat, var_ready, std_ready, done)

        @block.scalar
        def _(act):
            act.wait_ge(var_ready, 1)
            nc.scalar.activation(stat[:, 1, :], stat[:, 1, :], ACT.Sqrt).then_inc(std_ready, 1)


def final_norm(nc, t, out):
    with (
        nc.sbuf_tensor("stat2", [P, 2, WINDOWS], F32) as stat, nc.semaphore("stored_out") as stored, nc.semaphore("out_ready") as ready,
        nc.semaphore("norm_done2") as done, nc.semaphore("var_ready2") as var_ready, nc.semaphore("std_ready2") as std_ready,
        nc.Block() as block,
    ):
        sums = t["acc"][:, 0:WINDOWS * D].rearrange("p (w f) -> p w f", f=D)
        sq = t["xls"][:, :].bitcast(F32)[:, 0:WINDOWS * D].rearrange("p (w f) -> p w f", f=D)
        v = t["h"][:, :].rearrange("p (w f) -> p w f", f=D)
        parts = node_rows(out, v)

        @block.vector
        def _(dve):
            nc.vector.tensor_tensor(v, v, sums, ALU.add).then_inc(done, 1)
            dve.wait_ge(done, 1)
            normed(nc, dve, v, sq, stat, var_ready, std_ready, done)
            dve.sem_inc(ready, 1)

        @block.scalar
        def _(act):
            act.wait_ge(var_ready, 1)
            nc.scalar.activation(stat[:, 1, :], stat[:, 1, :], ACT.Sqrt).then_inc(std_ready, 1)

        @block.sync
        def _(sp):
            sp.wait_ge(done, 8)
            for rows, tile in parts:
                sp.dma_start(rows, tile).then_inc(stored, 16)
            sp.wait_ge(stored, 16 * len(parts))


def relations(nc, k, t, Wrel, recs, rel_table, wtab):
    with ExitStack() as ctx:
        def sb(name, shape, dt=F32):
            return ctx.enter_context(nc.sbuf_tensor(name, shape, dt))

        def sem(name):
            return ctx.enter_context(nc.semaphore(name))

        h, banks = t["h"], t["banks"]
        wrel = sb("wrel", [P, RELS, D])
        hs = sb("hs_r", [P, 2, 2 * D])
        hT = sb("hT_r", [P, 2, P])
        rec = sb("rec_r", [P, 2, GROUP, REC], I32)
        rows = sb("rows", [P, 8, D])
        hot = sb("hot_r", [P, 4, 4, P])
        prod = t["xls"][:, :].bitcast(F32)[:, 0:4 * RELS * D].rearrange("p (b a f) -> p b a f", b=2, a=2)
        ps_hT = [banks[i][:, 0:P] for i in range(2)]
        ps_s = [banks[i][:, 0:D] for i in range(4)]

        weights_loaded, zeroed, zero_row, acc_clear = sem("rel_weights"), sem("rel_zeroed"), sem("rel_zero_row"), sem("acc_clear")
        hs_ready, hT_ps, hT_ready = sem("hs_ready_r"), sem("hT_ps_r"), sem("hT_ready_r")
        prod_ps, prod_ready, stored = [sem(f"prod_ps{a}") for a in range(2)], [sem(f"prod_ready{a}") for a in range(2)], [sem(f"prod_stored{b}") for b in range(2)]
        rec_loaded = [sem("rec_loaded_r0"), sem("rec_loaded_r1")]
        gathered = [sem(f"gathered_r{i}") for i in range(8)]
        begun, hot_ready, s_ready, acc_done = sem("gather_begun_r"), sem("hot_ready_r"), sem("s_ready_r"), sem("acc_done_r")
        block = ctx.enter_context(nc.Block())
        PAIRS = WINDOWS // 2
        QUADS = SLOTS // 4

        @block.sync
        def _(sp):
            for a in range(2):
                sp.dma_start(wrel[a * D:a * D + D, :, :], Wrel.rearrange("r d f -> d r f")).then_inc(weights_loaded, 16)

            def store(j, b):
                for a in range(2):
                    sp.wait_ge(prod_ready[a], (j + 1) * 2)
                    sp.dma_start(rel_table[bass.ds((j * 2 + a) * (P * RELS), P * RELS), :].rearrange("(p r) f -> p (r f)", r=RELS),
                                 prod[:, b, a, :]).then_inc(stored[b], 16)

            with sp.Fori(0, PAIRS // 2) as n:
                for b in range(2):
                    store(n * 2 + b, b)
            store(PAIRS - 1, 0)

            def load(g, b, first):
                if not first:
                    sp.wait_ge(s_ready, (g - 1) * GROUP)
                sp.dma_start(rec[:, b, :, :].rearrange("p s r -> p (s r)"),
                             recs[bass.ds(g * GROUP * P, GROUP * P), :].rearrange("(p s) r -> p (s r)", s=GROUP)).then_inc(rec_loaded[b], 16)

            load(0, 0, True)
            load(1, 1, True)
            with sp.Fori(1, GROUPS // 2) as n:
                for b in range(2):
                    load(n * 2 + b, b, False)

        @block.gpsimd
        def _(pool):
            nc.gpsimd.memset(t["zeros"][0:1, :], 0.0).then_inc(zeroed, 1)
            pool.wait_ge(zeroed, 1)
            pool.dma_start(rel_table[PAD_NODE * RELS:PAD_NODE * RELS + 1, :], t["zeros"][0:1, 0:D]).then_inc(zero_row, 16)
            pool.wait_ge(zero_row, 16)
            pool.wait_ge(stored[0], 32 * (PAIRS // 2 + 1))
            pool.wait_ge(stored[1], 32 * (PAIRS // 2))

            def gather(n, i, first):
                if not first:
                    pool.wait_ge(s_ready, n * 16 + (i - 1) * 4)
                if i % 2 == 0:
                    pool.wait_ge(rec_loaded[i // 2], n * 16 + 16)
                pool.sem_inc(begun, 1)
                for s in range(4):
                    slot = i % 2 * 4 + s
                    nc.gpsimd.indirect_dma_start(
                        rows[:, slot, :], None, rel_table,
                        bass.IndirectOffsetOnAxis(ap=rec[:, i // 2, slot, 2:3], axis=0)).then_inc(gathered[slot], 16)

            for i in range(4):
                gather(0, i, i < 2)
            with pool.Fori(1, QUADS // 4) as n:
                for i in range(4):
                    gather(n, i, False)

        @block.scalar
        def _(act):
            def pair(j, b, first):
                if not first:
                    act.wait_ge(hT_ps, j - 1)
                nc.scalar.activation(hs[:, b, :], h[:, bass.ds(j * (2 * D), 2 * D)], ACT.Copy).then_inc(hs_ready, 1)
                act.wait_ge(hT_ps, j + 1)
                if not first:
                    act.wait_ge(prod_ps[1], (j - 1) * 2)
                nc.scalar.activation(hT[:, b, :], ps_hT[b], ACT.Copy).then_inc(hT_ready, 1)

            def evacuate(j, b, first):
                if not first:
                    act.wait_ge(stored[b], (j // 2) * 32)
                for n in range(2):
                    act.wait_ge(prod_ps[0], j * 2 + n + 1)
                    nc.scalar.activation(prod[:, b, 0, n * 512:n * 512 + 512], banks[2 + n][:, :], ACT.Copy).then_inc(prod_ready[0], 1)

            pair(0, 0, True)
            pair(1, 1, True)
            evacuate(0, 0, True)
            pair(2, 0, False)
            evacuate(1, 1, True)
            with act.Fori(1, PAIRS // 2) as n:
                pair(n * 2 + 1, 1, False)
                evacuate(n * 2, 0, False)
                pair(n * 2 + 2, 0, False)
                evacuate(n * 2 + 1, 1, False)
            evacuate(PAIRS - 1, 0, False)

        @block.tensor
        def _(pe):
            def turn(j, b):
                pe.wait_ge(hs_ready, j + 1)
                nc.tensor.transpose(ps_hT[b], hs[:, b, :], k["ident"][:, :]).then_inc(hT_ps, 1)

            def project(j, b, first):
                pe.wait_ge(hT_ready, j + 1)
                for n in range(2):
                    for a in range(2):
                        half = slice(a * D, a * D + D)
                        if not first:
                            pe.wait_ge(prod_ready[a], j * 2 + n - 1)
                        nc.tensor.matmul(banks[2 + 2 * a + n][:, :], hT[half, b, :], wrel[half, n * 8:n * 8 + 8, :].rearrange("p r f -> p (r f)"),
                                         start=True, stop=True).then_inc(prod_ps[a], 1)

            pe.wait_ge(weights_loaded, 32)
            turn(0, 0)
            turn(1, 1)
            project(0, 0, True)
            turn(2, 0)
            project(1, 1, False)
            with pe.Fori(1, PAIRS // 2) as n:
                turn(n * 2 + 1, 1)
                project(n * 2, 0, False)
                turn(n * 2 + 2, 0)
                project(n * 2 + 1, 1, False)
            project(PAIRS - 1, 0, False)

            def tile(n, i, first):
                if i % 4 == 0:
                    pe.wait_ge(hot_ready, n * 4 + (i // 4 + 1))
                pe.wait_ge(gathered[i % 8], n * 32 + (i // 8 + 1) * 16)
                if not (first and i < 4):
                    pe.wait_ge(acc_done, n * 16 + (i - 3))
                nc.tensor.matmul(ps_s[i % 4], hot[:, i // 4, i % 4, :], rows[:, i % 8, :], start=True, stop=True).then_inc(s_ready, 1)

            for i in range(16):
                tile(0, i, True)
            with pe.Fori(1, SLOTS // 16) as n:
                for i in range(16):
                    tile(n, i, False)

        @block.vector
        def _(dve):
            acc = t["acc"]
            nc.vector.memset(acc[:, 0:BINS * D], 0.0).then_inc(acc_clear, 1)

            def evacuate(j, b, first):
                if not first:
                    dve.wait_ge(stored[b], (j // 2) * 32)
                for n in range(2):
                    dve.wait_ge(prod_ps[1], j * 2 + n + 1)
                    nc.vector.tensor_copy(prod[:, b, 1, n * 512:n * 512 + 512], banks[4 + n][:, :]).then_inc(prod_ready[1], 1)

            evacuate(0, 0, True)
            evacuate(1, 1, True)
            with dve.Fori(1, PAIRS // 2) as n:
                for b in range(2):
                    evacuate(n * 2 + b, b, False)
            evacuate(PAIRS - 1, 0, False)
            dve.wait_ge(acc_clear, 1)

            def one_hots(n, q, first):
                dve.wait_ge(rec_loaded[q // 2], n * 16 + 16)
                if not first:
                    dve.wait_ge(s_ready, n * 16 + (q - 3) * 4)
                place = rec[:, q // 2, q % 2 * 4:q % 2 * 4 + 4, 1:2].bitcast(F32).to_broadcast([P, 4, P])
                nc.vector.tensor_tensor(hot[:, q, :, :], k["col"][:, :].unsqueeze(1).to_broadcast([P, 4, P]), place,
                                        ALU.is_equal).then_inc(hot_ready, 1)

            def sums(n, i):
                _, ws = nc.values_load_multi_w_load_instructions(
                    wtab[0:1, bass.ds(n * 16 + i * 4, 4)], engines=[mybir.EngineType.DVE], min_val=0, max_val=BINS - 1,
                    skip_runtime_bounds_check_because="the window of a slot is counted over BINS windows and capped there")
                for s in range(4):
                    at = i * 4 + s
                    dve.wait_ge(s_ready, n * 16 + at + 1)
                    dve.wait_ge(acc_done, n * 16 + at)
                    a = acc[:, bass.ds(ws[s] * D, D)]
                    nc.vector.tensor_tensor(a, a, ps_s[at % 4], ALU.add).then_inc(acc_done, 1)

            one_hots(0, 0, True)
            for i in range(4):
                if i < 3:
                    one_hots(0, i + 1, True)
                sums(0, i)
            with dve.Fori(1, SLOTS // 16) as n:
                for i in range(4):
                    one_hots(n, i, False)
                    sums(n, i)


def gnn(nc, x, src, dst, rel, W, b, attn, Wr, Wrel, out):
    recs = nc.dram_tensor("recs", [SLOTS * P, REC], I32, kind="Internal").ap()
    wtab_dram = nc.dram_tensor("wtab_dram", [SLOTS], I32, kind="Internal").ap()
    rel_table = nc.dram_tensor("rel_table", [PAD_NODE * RELS + 1, D], F32, kind="Internal").ap()
    table = nc.dram_tensor("table", [PAD_NODE + 1, HF], F32, kind="Internal").ap()
    with ExitStack() as ctx:
        def sb(name, shape, dt):
            return ctx.enter_context(nc.sbuf_tensor(name, shape, dt))

        k = {
            "col": sb("col", [P, P], F32),
            "col_bf": sb("col_bf", [P, P], BF16),
            "lane": sb("lane", [P, 1], F32),
            "slot_id": sb("slot_id", [P, SLOTS // P], F32),
            "ones": sb("ones", [P, P], F32),
            "ones_bf": sb("ones_bf", [P, P], BF16),
            "ident": sb("ident", [P, P], F32),
            "ident_bf": sb("ident_bf", [P, P], BF16),
            "before": sb("before", [P, P], BF16),
        }
        wtab = sb("wtab", [1, SLOTS], I32)
        constants(nc, k)
        order_edges(nc, k, src, dst, rel, recs, wtab_dram, wtab)
        t = {
            "h": sb("h", [P, WINDOWS * D], F32),
            "acc": sb("acc", [P, BINS * HEADS * (D + 1)], F32),
            "xls": sb("xls", [P, BINS * 3 * HF], BF16),
            "zeros": sb("zeros", [1, HF], F32),
            "banks": [ctx.enter_context(nc.psum_tensor(f"bank{i}", [P, 512], F32)) for i in range(8)],
        }
        load_nodes(nc, x, t["h"])
        attention_layers(nc, k, t, x, W, b, attn, Wr, recs, table, wtab)
        residual_norm(nc, t, x)
        relations(nc, k, t, Wrel, recs, rel_table, wtab)
        final_norm(nc, t, out)


_INS = ["x", "src", "dst", "edge_type_16", "L0_gnn_W", "L0_gnn_b", "L0_gnn_attn", "L0_gnn_Wr", "L1_gnn_weight"]


def kernel(**inputs):
    import numpy as _np
    import concourse.bacc as _bacc
    from concourse import mybir as _mybir
    from concourse.bass_utils import run_bass_kernel_spmd as _run

    nc = _bacc.Bacc("TRN2", target_bir_lowering=False, num_devices=1)
    arrays, args = {}, []
    for name in _INS:
        a = _np.ascontiguousarray(inputs[name])
        arrays[f"in_{name}"] = a
        args.append(nc.dram_tensor(f"in_{name}", a.shape, _mybir.dt.from_np(a.dtype), kind="ExternalInput").ap())
    args.append(nc.dram_tensor("out_0", (NODES, D), F32, kind="ExternalOutput").ap())
    gnn(nc, *args)
    r = _run(nc, [arrays], core_ids=[0])
    return r.results[0]["out_0"]
```
